# Optimizing a Trainium2 kernel written in Bass

```python
import numpy as np
import jax
import jax.numpy as jnp

def _softmax(x, axis=-1):
    return jax.nn.softmax(x, axis=axis)

def _gelu(x):
    return jax.nn.gelu(x, approximate=True)

def _silu(x):
    return jax.nn.silu(x)

def _sigmoid(x):
    return jax.nn.sigmoid(x)

def _layernorm(x, axis=-1, eps=1e-05):
    m = jnp.mean(x, axis=axis, keepdims=True)
    v = jnp.var(x, axis=axis, keepdims=True)
    return (x - m) / jnp.sqrt(v + eps)

def _scatter_add(tgt, idx, src, axis=0):
    return tgt.at[idx].add(src)

def _segment_sum(src, seg, n):
    return jax.ops.segment_sum(src, seg, n)
kernel_name = 'mk_dlrm_tower_d1_rec_r8_b840f8'

def setup_inputs(seed: int=0):
    np.random.seed(seed)
    _w = jnp.asarray

    def _rec_inputs():
        import jax
        import jax.numpy as jnp
        _tk = jax.random.key(seed)
        dense_ctx = jax.random.normal(jax.random.fold_in(_tk, 190), (512, 16), jnp.float32)
        ids = jnp.stack([jax.random.randint(jax.random.fold_in(_tk, 200 + f), (512,), 0, v, jnp.int32) for f, v in enumerate([12500, 125000, 1250, 12500, 12500, 12500, 1250, 1000, 1000, 12500, 1250, 1250, 12500, 1250, 1000, 12500, 1250, 12500, 1000, 1250, 1250, 1000, 1000, 1250, 1000, 1000, 1000])], axis=1)
        tbl_0 = 0.05 * jax.random.normal(jax.random.fold_in(_tk, 500 + 0), (12500, 128), jnp.float32)
        tbl_1 = 0.05 * jax.random.normal(jax.random.fold_in(_tk, 500 + 1), (125000, 128), jnp.float32)
        tbl_2 = 0.05 * jax.random.normal(jax.random.fold_in(_tk, 500 + 2), (1250, 128), jnp.float32)
        tbl_3 = 0.05 * jax.random.normal(jax.random.fold_in(_tk, 500 + 3), (12500, 128), jnp.float32)
        tbl_4 = 0.05 * jax.random.normal(jax.random.fold_in(_tk, 500 + 4), (12500, 128), jnp.float32)
        tbl_5 = 0.05 * jax.random.normal(jax.random.fold_in(_tk, 500 + 5), (12500, 128), jnp.float32)
        tbl_6 = 0.05 * jax.random.normal(jax.random.fold_in(_tk, 500 + 6), (1250, 128), jnp.float32)
        tbl_7 = 0.05 * jax.random.normal(jax.random.fold_in(_tk, 500 + 7), (1000, 128), jnp.float32)
        tbl_8 = 0.05 * jax.random.normal(jax.random.fold_in(_tk, 500 + 8), (1000, 128), jnp.float32)
        tbl_9 = 0.05 * jax.random.normal(jax.random.fold_in(_tk, 500 + 9), (12500, 128), jnp.float32)
        tbl_10 = 0.05 * jax.random.normal(jax.random.fold_in(_tk, 500 + 10), (1250, 128), jnp.float32)
        tbl_11 = 0.05 * jax.random.normal(jax.random.fold_in(_tk, 500 + 11), (1250, 128), jnp.float32)
        tbl_12 = 0.05 * jax.random.normal(jax.random.fold_in(_tk, 500 + 12), (12500, 128), jnp.float32)
        tbl_13 = 0.05 * jax.random.normal(jax.random.fold_in(_tk, 500 + 13), (1250, 128), jnp.float32)
        tbl_14 = 0.05 * jax.random.normal(jax.random.fold_in(_tk, 500 + 14), (1000, 128), jnp.float32)
        tbl_15 = 0.05 * jax.random.normal(jax.random.fold_in(_tk, 500 + 15), (12500, 128), jnp.float32)
        tbl_16 = 0.05 * jax.random.normal(jax.random.fold_in(_tk, 500 + 16), (1250, 128), jnp.float32)
        tbl_17 = 0.05 * jax.random.normal(jax.random.fold_in(_tk, 500 + 17), (12500, 128), jnp.float32)
        tbl_18 = 0.05 * jax.random.normal(jax.random.fold_in(_tk, 500 + 18), (1000, 128), jnp.float32)
        tbl_19 = 0.05 * jax.random.normal(jax.random.fold_in(_tk, 500 + 19), (1250, 128), jnp.float32)
        tbl_20 = 0.05 * jax.random.normal(jax.random.fold_in(_tk, 500 + 20), (1250, 128), jnp.float32)
        tbl_21 = 0.05 * jax.random.normal(jax.random.fold_in(_tk, 500 + 21), (1000, 128), jnp.float32)
        tbl_22 = 0.05 * jax.random.normal(jax.random.fold_in(_tk, 500 + 22), (1000, 128), jnp.float32)
        tbl_23 = 0.05 * jax.random.normal(jax.random.fold_in(_tk, 500 + 23), (1250, 128), jnp.float32)
        tbl_24 = 0.05 * jax.random.normal(jax.random.fold_in(_tk, 500 + 24), (1000, 128), jnp.float32)
        tbl_25 = 0.05 * jax.random.normal(jax.random.fold_in(_tk, 500 + 25), (1000, 128), jnp.float32)
        tbl_26 = 0.05 * jax.random.normal(jax.random.fold_in(_tk, 500 + 26), (1000, 128), jnp.float32)
        _rk = jax.random.fold_in(_tk, 7)
        W_top1 = 0.0161733 * jax.random.normal(jax.random.fold_in(_tk, 801), (3823, 512), jnp.float32)
        W_top2 = 0.0441942 * jax.random.normal(jax.random.fold_in(_tk, 802), (512, 256), jnp.float32)
        W_top3 = 0.0625 * jax.random.normal(jax.random.fold_in(_tk, 803), (256, 1), jnp.float32)
        b_top1 = jnp.zeros((512,), jnp.float32)
        b_top2 = jnp.zeros((256,), jnp.float32)
        return (dense_ctx, ids, tbl_0, tbl_1, tbl_2, tbl_3, tbl_4, tbl_5, tbl_6, tbl_7, tbl_8, tbl_9, tbl_10, tbl_11, tbl_12, tbl_13, tbl_14, tbl_15, tbl_16, tbl_17, tbl_18, tbl_19, tbl_20, tbl_21, tbl_22, tbl_23, tbl_24, tbl_25, tbl_26, W_top1, b_top1, W_top2, b_top2, W_top3)
    dense_ctx, ids, tbl_0, tbl_1, tbl_2, tbl_3, tbl_4, tbl_5, tbl_6, tbl_7, tbl_8, tbl_9, tbl_10, tbl_11, tbl_12, tbl_13, tbl_14, tbl_15, tbl_16, tbl_17, tbl_18, tbl_19, tbl_20, tbl_21, tbl_22, tbl_23, tbl_24, tbl_25, tbl_26, W_top1, b_top1, W_top2, b_top2, W_top3 = _rec_inputs()

    def _L0_rec_setup():
        import jax, jax.numpy as jnp
        import numpy as np
        NUM_FEATURES = 27
        FEATURE_DIM = 128
        BATCH = 2048
        _TRIU_I, _TRIU_J = np.triu_indices(NUM_FEATURES, k=1)
        key = jax.random.key(seed)
        embeddings = jax.random.normal(key, (BATCH, NUM_FEATURES, FEATURE_DIM), dtype=jnp.float32)
        return {'embeddings': embeddings}
    _L0_rec_all = _L0_rec_setup()
    _L0_rec_in = {k: v for k, v in _L0_rec_all.items() if k in ()}
    del _L0_rec_all
    return {'dense_ctx': dense_ctx, 'ids': ids, 'tbl_0': tbl_0, 'tbl_1': tbl_1, 'tbl_2': tbl_2, 'tbl_3': tbl_3, 'tbl_4': tbl_4, 'tbl_5': tbl_5, 'tbl_6': tbl_6, 'tbl_7': tbl_7, 'tbl_8': tbl_8, 'tbl_9': tbl_9, 'tbl_10': tbl_10, 'tbl_11': tbl_11, 'tbl_12': tbl_12, 'tbl_13': tbl_13, 'tbl_14': tbl_14, 'tbl_15': tbl_15, 'tbl_16': tbl_16, 'tbl_17': tbl_17, 'tbl_18': tbl_18, 'tbl_19': tbl_19, 'tbl_20': tbl_20, 'tbl_21': tbl_21, 'tbl_22': tbl_22, 'tbl_23': tbl_23, 'tbl_24': tbl_24, 'tbl_25': tbl_25, 'tbl_26': tbl_26, 'W_top1': W_top1, 'b_top1': b_top1, 'W_top2': W_top2, 'b_top2': b_top2, 'W_top3': W_top3}

def reference(dense_ctx, ids, tbl_0, tbl_1, tbl_2, tbl_3, tbl_4, tbl_5, tbl_6, tbl_7, tbl_8, tbl_9, tbl_10, tbl_11, tbl_12, tbl_13, tbl_14, tbl_15, tbl_16, tbl_17, tbl_18, tbl_19, tbl_20, tbl_21, tbl_22, tbl_23, tbl_24, tbl_25, tbl_26, W_top1, b_top1, W_top2, b_top2, W_top3):
    import jax
    import jax.numpy as jnp

    def _L0_rec_ref(embeddings):
        import jax, jax.numpy as jnp
        import numpy as np
        NUM_FEATURES = 27
        FEATURE_DIM = 128
        BATCH = 2048
        _TRIU_I, _TRIU_J = np.triu_indices(NUM_FEATURES, k=1)
        B = embeddings.shape[0]
        interactions = jnp.einsum('bfd,bgd->bfg', embeddings, embeddings)
        flat_interactions = interactions[:, _TRIU_I, _TRIU_J]
        flat_embeddings = embeddings.reshape(B, -1)
        return jnp.concatenate([flat_embeddings, flat_interactions], axis=1)
    e = jnp.stack([tbl_0[ids[:, 0]], tbl_1[ids[:, 1]], tbl_2[ids[:, 2]], tbl_3[ids[:, 3]], tbl_4[ids[:, 4]], tbl_5[ids[:, 5]], tbl_6[ids[:, 6]], tbl_7[ids[:, 7]], tbl_8[ids[:, 8]], tbl_9[ids[:, 9]], tbl_10[ids[:, 10]], tbl_11[ids[:, 11]], tbl_12[ids[:, 12]], tbl_13[ids[:, 13]], tbl_14[ids[:, 14]], tbl_15[ids[:, 15]], tbl_16[ids[:, 16]], tbl_17[ids[:, 17]], tbl_18[ids[:, 18]], tbl_19[ids[:, 19]], tbl_20[ids[:, 20]], tbl_21[ids[:, 21]], tbl_22[ids[:, 22]], tbl_23[ids[:, 23]], tbl_24[ids[:, 24]], tbl_25[ids[:, 25]], tbl_26[ids[:, 26]]], axis=1)
    z = _L0_rec_ref(e)
    z = z.reshape(z.shape[0], -1)
    h = jnp.concatenate([z, dense_ctx], axis=1)
    h = jnp.maximum(h @ W_top1 + b_top1, 0.0)
    h = jnp.maximum(h @ W_top2 + b_top2, 0.0)
    y = h @ W_top3
    return y

_drawn_inputs = setup_inputs


def setup_inputs(seed=0):
    import zlib

    import numpy as np

    out = dict(_drawn_inputs(seed))
    spreads = {'b_top1': (0.0, 0.1), 'b_top2': (0.0, 0.1)}
    factors = {}
    for name, (base, spread) in spreads.items():
        noise = np.random.default_rng([zlib.crc32(name.encode()), seed]).standard_normal(out[name].shape)
        drawn = base * np.exp(spread * noise) if base else spread * noise
        out[name] = jnp.asarray(drawn.astype(out[name].dtype))
    for name, factor in factors.items():
        out[name] = (out[name] * factor).astype(out[name].dtype)
    return out
```

```python
import concourse.bass as bass
from concourse import mybir
from contextlib import ExitStack

P = 128
B, F, D = 512, 27, 128
NDENSE = 16
H1, H2 = 512, 256
T = B // P
GF = 3
G = F // GF
RING = 3
LAG = 5
KOFF = (F - 1) // 2
ZF = 9
ZROWS = ZF * KOFF
NZ = F // ZF
NW = F + NZ + 1
AUX = NW - 1
QUAD = 32
HALF = QUAD // 2
FX = F + KOFF
ETI = P * F + QUAD - F


def build(nc, ids, tables, w1_emb, w1_int, w1_dense, b1, w2, b2, w3, dense_t, scratch, out):
    fp32, fp32r, u32 = mybir.dt.float32, mybir.dt.float32r, mybir.dt.uint32
    ACT = mybir.ActivationFunctionType
    ALU = mybir.AluOpType
    ctx = ExitStack()
    with ctx:
        def sb(name, shape, dt=fp32):
            return ctx.enter_context(nc.sbuf_tensor(name, shape, dt))

        def bank(name):
            return ctx.enter_context(nc.psum_tensor(name, [P, 512], fp32))

        def sem(name):
            return ctx.enter_context(nc.semaphore(name))

        idx = sb("idx", [P, T, F], u32)
        ident = sb("ident", [P, P])
        rows = sb("rows", [P, RING, GF, D])
        emb = sb("emb", [P, RING, GF, P])
        emb_hi = sb("emb_hi", [P, G, GF, P], fp32r)
        emb_lo = sb("emb_lo", [P, G, GF, P], fp32r)
        emb_bf = sb("emb_bf", [P, ETI])
        w_hi = sb("w_hi", [P, NW, H1], fp32r)
        w_lo = sb("w_lo", [P, NW, H1], fp32r)
        w_raw = sb("w_raw", [P, 2, GF * H1])
        dots = w_raw[:, 0, 0:FX * QUAD].rearrange("p (g i) -> p g i", g=FX)
        h1 = w_raw[:, 1, 0:H1]
        z = sb("z", [P, NZ + 1, P])
        z_hi = sb("z_hi", [P, NZ + 1, P], fp32r)
        z_lo = sb("z_lo", [P, NZ + 1, P], fp32r)
        w2_sb = sb("w2_sb", [P, H1 // P, H2])
        b2_sb = sb("b2_sb", [P, H2 // P])
        w3_sb = sb("w3_sb", [P, H2 // P])
        h1_t = sb("h1_t", [P, H1 // P, P])
        h2_t = sb("h2_t", [P, H2 // P, P])
        y = sb("y", [1, B])

        tr_ps = [bank(f"tr_ps{i}") for i in range(RING)]
        dot_ps = [bank(f"dot_ps{i}") for i in range(2)]
        h1_ps = bank("h1_ps")
        h1t_ps = bank("h1t_ps")
        h2_ps = bank("h2_ps")

        ids_loaded = sem("ids_loaded")
        const_loaded = sem("const_loaded")
        ident_zeroed = sem("ident_zeroed")
        ident_ready = sem("ident_ready")
        pads_ready = sem("pads_ready")
        z_zeroed = sem("z_zeroed")
        gathered = [sem(f"gathered{i}") for i in range(RING)]
        transposed = sem("transposed")
        emb_ready = sem("emb_ready")
        emb_bf_ready = sem("emb_bf_ready")
        hi_ready = sem("hi_ready")
        split_ready = sem("split_ready")
        group_summed = sem("group_summed")
        w_loaded = [sem(f"w_loaded{i}") for i in range(2)]
        w_hi_ready = sem("w_hi_ready")
        w_lo_ready = sem("w_lo_ready")
        dots_done = sem("dots_done")
        dots_copied = sem("dots_copied")
        dots_stored = sem("dots_stored")
        dense_loaded = sem("dense_loaded")
        z_loaded = sem("z_loaded")
        z_hi_ready = sem("z_hi_ready")
        z_ready = sem("z_ready")
        h1_done = sem("h1_done")
        h1_ready = sem("h1_ready")
        h1t_done = sem("h1t_done")
        h1t_ready = sem("h1t_ready")
        h2_done = sem("h2_done")
        h2_ready = sem("h2_ready")
        y_done = sem("y_done")
        y_ready = sem("y_ready")
        out_stored = sem("out_stored")

        block = ctx.enter_context(nc.Block())

        W_LOADS = G + 2

        @block.sync
        def _(sp):
            sp.dma_start(idx[:], ids.rearrange("(t p) f -> p t f", p=P)).then_inc(ids_loaded, 16)

            def load_w(n):
                if n >= 2:
                    sp.wait_ge(w_hi_ready, n - 1)
                    sp.wait_ge(w_lo_ready, n - 1)
                slot, done = w_raw[:, n % 2, :], w_loaded[n % 2]
                if n < G:
                    src = w1_emb[n * GF * D:(n + 1) * GF * D, :].rearrange("(f k) n -> k f n", f=GF)
                    sp.dma_start(slot.rearrange("k (f n) -> k f n", f=GF), src).then_inc(done, 16)
                elif n == G:
                    src = w1_int.rearrange("(z k) n -> k z n", z=NZ)
                    sp.dma_start(slot[0:ZROWS, :].rearrange("k (z n) -> k z n", z=NZ), src).then_inc(done, 16)
                else:
                    sp.dma_start(slot[0:1, 0:H1], b1).then_inc(done, 16)
                    sp.dma_start(slot[1:1 + NDENSE, 0:H1], w1_dense).then_inc(done, 16)

            load_w(0)
            load_w(1)
            sp.dma_start(w2_sb[:], w2.rearrange("(c k) n -> k c n", c=H1 // P)).then_inc(const_loaded, 16)
            with nc.allow_non_contiguous_dma(reason="256 biases and 256 weights onto partitions"):
                sp.dma_start(b2_sb[:], b2).then_inc(const_loaded, 16)
                sp.dma_start(w3_sb[:], w3).then_inc(const_loaded, 16)
            sp.wait_ge(z_zeroed, 2)
            sp.dma_start(z[1:1 + NDENSE, NZ, :], dense_t[:, 0:P]).then_inc(dense_loaded, 16)
            for n in range(2, W_LOADS):
                load_w(n)
            for t in range(T):
                sp.wait_ge(dots_copied, 2 * (t + 1))
                if t > 0:
                    sp.wait_ge(z_loaded, 16 * NZ * 4 * t)
                sp.dma_start(scratch[:, 0:F * QUAD], dots[:, 0:F, :].rearrange("p g i -> p (g i)")).then_inc(dots_stored, 16)
                sp.dma_start(scratch[:, F * QUAD:FX * QUAD],
                             dots[:, 0:KOFF, :].rearrange("p g i -> p (g i)")).then_inc(dots_stored, 16)
                if t > 0:
                    sp.wait_ge(z_ready, t)
                    sp.dma_start(z[1:1 + NDENSE, NZ, :], dense_t[:, t * P:(t + 1) * P]).then_inc(dense_loaded, 16)
                sp.wait_ge(dots_stored, 32 * (t + 1))
                for zt in range(NZ):
                    for j in range(4):
                        src = bass.AP(tensor=scratch.tensor, offset=(QUAD * j + ZF * zt) * FX * QUAD + (ZF * zt + 1) * QUAD,
                                      ap=[[FX * QUAD + QUAD, ZF], [QUAD, KOFF], [1, QUAD]])
                        sp.dma_start(z[0:ZROWS, zt, j * QUAD:(j + 1) * QUAD], src).then_inc(z_loaded, 16)
            sp.wait_ge(y_ready, T)
            sp.dma_start(out, y[:]).then_inc(out_stored, 16)
            sp.wait_ge(out_stored, 16)

        @block.gpsimd
        def _(pool):
            nc.gpsimd.memset(ident[:], 0.0).then_inc(ident_zeroed, 1)
            pool.wait_ge(ident_zeroed, 1)
            nc.gpsimd.affine_select(out=ident[:], in_=ident[:], compare_op=ALU.not_equal, fill=1.0, base=0,
                                    pattern=[[-1, P]], channel_multiplier=1).then_inc(ident_ready, 1)
            pool.wait_ge(ids_loaded, 16)
            for t in range(T):
                for g in range(G):
                    if t * G + g >= RING:
                        pool.wait_ge(transposed, t * G + g - RING + 1)
                    for c in range(GF):
                        f = g * GF + c
                        nc.gpsimd.indirect_dma_start(
                            out=rows[:, g % RING, c, :], out_offset=None, in_=tables[f][:, :],
                            in_offset=bass.IndirectOffsetOnAxis(ap=idx[:, t, f:f + 1], axis=0),
                        ).then_inc(gathered[g % RING], 16)

        @block.scalar
        def _(act):
            def sample_major(t, g):
                n = t * G + g
                act.wait_ge(emb_ready, n + 1)
                if g == 0 and t > 0:
                    act.wait_ge(dots_done, 2 * t)
                dst = emb_bf[:, 0:P * F].rearrange("p (b f) -> p b f", f=F)[:, :, g * GF:(g + 1) * GF]
                nc.scalar.activation(dst, emb[:, g % RING, :, :].rearrange("p f b -> p b f"),
                                     ACT.Copy).then_inc(emb_bf_ready, 1)

            def split_w_hi(n):
                act.wait_ge(w_loaded[n % 2], 16 * (n // 2 + 1) if n < W_LOADS - 1 else 16 * (n // 2 + 2))
                k = P if n < G else ZROWS if n == G else 1 + NDENSE
                c = GF if n <= G else 1
                nc.scalar.activation(w_hi[0:k, n * GF:n * GF + c, :].rearrange("k f n -> k (f n)"),
                                     w_raw[0:k, n % 2, 0:c * H1], ACT.Copy).then_inc(w_hi_ready, 1)

            def finish_h1(t):
                act.wait_ge(h1_done, t + 1)
                if t > 0:
                    act.wait_ge(h1t_done, t)
                nc.scalar.activation(h1, h1_ps[:], ACT.Relu).then_inc(h1_ready, 1)

            def finish_h2(t):
                act.wait_ge(h2_done, t + 1)
                if t > 0:
                    act.wait_ge(y_done, t)
                if t == 0:
                    act.wait_ge(const_loaded, 48)
                for m in range(H2 // P):
                    nc.scalar.activation(h2_t[:, m, :], h2_ps[:, m * P:(m + 1) * P], ACT.Relu,
                                         bias=b2_sb[:, m:m + 1]).then_inc(h2_ready, 1)

            for t in range(T):
                for g in range(G):
                    n = t * G + g
                    act.wait_ge(transposed, n + 1)
                    if n >= RING:
                        act.wait_ge(split_ready, n - RING + 1)
                        act.wait_ge(emb_bf_ready, n - RING + 1)
                    nc.scalar.activation(emb[:, g % RING, :, :].rearrange("p f b -> p (f b)"),
                                         tr_ps[g % RING][:, 0:GF * P], ACT.Copy).then_inc(emb_ready, 1)
                    if t == 0:
                        split_w_hi(g)
                    if g > 0:
                        sample_major(t, g - 1)
                    if g == G - 1:
                        sample_major(t, g)
                        if t == 0:
                            split_w_hi(G)
                            split_w_hi(G + 1)
                    if t > 0 and g == LAG:
                        finish_h1(t - 1)
                    if t > 0 and g == LAG + 2:
                        finish_h2(t - 1)
            finish_h1(T - 1)
            finish_h2(T - 1)

        @block.vector
        def _(dve):
            nc.vector.memset(z[:, NZ, :], 0.0).then_inc(z_zeroed, 1)
            dve.wait_ge(z_zeroed, 1)
            nc.vector.memset(z[0:1, NZ, :], 1.0).then_inc(z_zeroed, 1)
            nc.vector.memset(emb_bf[:, P * F:ETI], 0.0).then_inc(pads_ready, 1)

            def split(t, g):
                n = t * G + g
                dve.wait_ge(emb_ready, n + 1)
                if t > 0:
                    dve.wait_ge(group_summed, n - G + 1)
                nc.vector.tensor_copy(emb_hi[:, g, :, :], emb[:, g % RING, :, :]).then_inc(hi_ready, 1)
                dve.wait_ge(hi_ready, n + 1)
                nc.vector.tensor_tensor(emb_lo[:, g, :, :], emb[:, g % RING, :, :], emb_hi[:, g, :, :].bitcast(fp32),
                                        ALU.subtract).then_inc(split_ready, 1)

            def split_w_lo(n):
                dve.wait_ge(w_hi_ready, n + 1)
                k = P if n < G else ZROWS if n == G else 1 + NDENSE
                c = GF if n <= G else 1
                tiles = slice(n * GF, n * GF + c)
                nc.vector.tensor_tensor(w_lo[0:k, tiles, :].rearrange("k f n -> k (f n)"), w_raw[0:k, n % 2, 0:c * H1],
                                        w_hi[0:k, tiles, :].rearrange("k f n -> k (f n)").bitcast(fp32),
                                        ALU.subtract).then_inc(w_lo_ready, 1)

            def copy_dots(t):
                if t == 0:
                    dve.wait_ge(w_lo_ready, W_LOADS)
                else:
                    dve.wait_ge(dots_stored, 32 * t)
                for h in range(2):
                    dve.wait_ge(dots_done, 2 * t + h + 1)
                    nc.vector.tensor_copy(
                        dots[:, 0:F, h * HALF:(h + 1) * HALF],
                        dot_ps[h][:, 0:HALF * F].rearrange("p (i g) -> p g i", g=F)).then_inc(dots_copied, 1)

            def split_z(t):
                dve.wait_ge(z_loaded, 16 * NZ * 4 * (t + 1))
                dve.wait_ge(dense_loaded, 16 * (t + 1))
                if t > 0:
                    dve.wait_ge(h1_done, t)
                nc.vector.tensor_copy(z_hi[0:ZROWS], z[0:ZROWS]).then_inc(z_hi_ready, 1)
                dve.wait_ge(z_hi_ready, t + 1)
                nc.vector.tensor_tensor(z_lo[0:ZROWS], z[0:ZROWS], z_hi[0:ZROWS].bitcast(fp32),
                                        ALU.subtract).then_inc(z_ready, 1)

            def copy_h1t(t):
                dve.wait_ge(h1t_done, t + 1)
                if t > 0:
                    dve.wait_ge(h2_done, t)
                nc.vector.tensor_copy(h1_t[:].rearrange("p c b -> p (c b)"), h1t_ps[:]).then_inc(h1t_ready, 1)

            def copy_y(t):
                dve.wait_ge(y_done, t + 1)
                nc.vector.tensor_copy(y[0:1, t * P:(t + 1) * P], h2_ps[0:1, H2:H2 + P]).then_inc(y_ready, 1)

            for t in range(T):
                for g in range(G):
                    split(t, g)
                    if t == 0:
                        split_w_lo(g)
                        if g == G - 1:
                            split_w_lo(G)
                            split_w_lo(G + 1)
                    if t > 0:
                        if g == 0:
                            copy_dots(t - 1)
                        if g == LAG - 1:
                            split_z(t - 1)
                        if g == LAG + 1:
                            copy_h1t(t - 1)
                        if g == LAG + 3:
                            copy_y(t - 1)
            copy_dots(T - 1)
            split_z(T - 1)
            copy_h1t(T - 1)
            copy_y(T - 1)

        @block.tensor
        def _(pe):
            def transpose_group(t, g):
                n = t * G + g
                pe.wait_ge(gathered[g % RING], 16 * GF * (t * (G // RING) + g // RING + 1))
                if n >= RING:
                    pe.wait_ge(emb_ready, n - RING + 1)
                for c in range(GF):
                    last = nc.tensor.transpose(tr_ps[g % RING][:, c * P:(c + 1) * P], rows[:, g % RING, c, :], ident[:])
                last.then_inc(transposed, 1)

            def interact(t):
                pe.wait_ge(emb_bf_ready, G * (t + 1))
                if t > 0:
                    pe.wait_ge(dots_copied, 2 * t)
                for h in range(2):
                    for i in range(h * HALF, (h + 1) * HALF):
                        for j in range(4):
                            b = (QUAD * j + i) * F
                            last = nc.tensor.matmul(
                                dot_ps[h][QUAD * j:QUAD * (j + 1), (i - h * HALF) * F:(i - h * HALF + 1) * F],
                                emb_bf[:, b:b + QUAD], emb_bf[:, b:b + F], start=True, stop=True)
                    last.then_inc(dots_done, 1)

            def three_products(hi, lo, k, w, start, stop):
                nc.tensor.matmul(h1_ps[:], hi, w_hi[0:k, w, :], start=start, stop=False)
                nc.tensor.matmul(h1_ps[:], hi, w_lo[0:k, w, :], start=False, stop=False)
                return nc.tensor.matmul(h1_ps[:], lo, w_hi[0:k, w, :], start=False, stop=stop)

            def sum_group(t, g):
                pe.wait_ge(split_ready, t * G + g + 1)
                if t == 0:
                    pe.wait_ge(w_lo_ready, g + 1)
                if g == 0 and t > 0:
                    pe.wait_ge(h1_ready, t)
                for c in range(GF):
                    last = three_products(emb_hi[:, g, c, :], emb_lo[:, g, c, :], P, g * GF + c,
                                          g == 0 and c == 0, False)
                last.then_inc(group_summed, 1)

            def sum_pairs_and_dense(t):
                pe.wait_ge(z_ready, t + 1)
                if t == 0:
                    pe.wait_ge(w_lo_ready, W_LOADS)
                for zt in range(NZ):
                    three_products(z_hi[0:ZROWS, zt, :], z_lo[0:ZROWS, zt, :], ZROWS, F + zt, False, False)
                three_products(z_hi[0:1 + NDENSE, NZ, :], z_lo[0:1 + NDENSE, NZ, :], 1 + NDENSE, AUX,
                               False, True).then_inc(h1_done, 1)

            def transpose_h1(t):
                pe.wait_ge(h1_ready, t + 1)
                if t > 0:
                    pe.wait_ge(h1t_ready, t)
                for c in range(H1 // P):
                    last = nc.tensor.transpose(h1t_ps[:, c * P:(c + 1) * P], h1[:, c * P:(c + 1) * P], ident[:])
                last.then_inc(h1t_done, 1)

            def second_layer(t):
                pe.wait_ge(h1t_ready, t + 1)
                if t == 0:
                    pe.wait_ge(const_loaded, 48)
                else:
                    pe.wait_ge(y_ready, t)
                for m in range(H2 // P):
                    for c in range(H1 // P):
                        last = nc.tensor.matmul(h2_ps[:, m * P:(m + 1) * P], w2_sb[:, c, m * P:(m + 1) * P],
                                                h1_t[:, c, :], start=c == 0, stop=c == H1 // P - 1)
                last.then_inc(h2_done, 1)

            def third_layer(t):
                pe.wait_ge(h2_ready, (H2 // P) * (t + 1))
                for m in range(H2 // P):
                    last = nc.tensor.matmul(h2_ps[0:1, H2:H2 + P], w3_sb[:, m:m + 1], h2_t[:, m, :],
                                            start=m == 0, stop=m == H2 // P - 1)
                last.then_inc(y_done, 1)

            pe.wait_ge(ident_ready, 1)
            for t in range(T):
                for g in range(G):
                    transpose_group(t, g)
                    if t > 0 and g == 0:
                        if t == 1:
                            pe.wait_ge(pads_ready, 1)
                        interact(t - 1)
                    if g >= LAG:
                        sum_group(t, g - LAG)
                    elif t > 0:
                        sum_group(t - 1, g - LAG + G)
                    if t > 0:
                        if g == LAG - 1:
                            sum_pairs_and_dense(t - 1)
                        if g == LAG:
                            transpose_h1(t - 1)
                        if g == LAG + 1:
                            second_layer(t - 1)
                        if g == LAG + 2:
                            third_layer(t - 1)
            interact(T - 1)
            for g in range(G - LAG, G):
                sum_group(T - 1, g)
            sum_pairs_and_dense(T - 1)
            transpose_h1(T - 1)
            second_layer(T - 1)
            third_layer(T - 1)


def kernel(**inputs):
    import numpy as np
    import concourse.bacc as bacc
    from concourse.bass_utils import run_bass_kernel_spmd as run

    nc = bacc.Bacc("TRN2", target_bir_lowering=False, num_devices=1)
    arrays = {}

    def dram(name, a):
        arrays[name] = a = np.ascontiguousarray(a)
        return nc.dram_tensor(name, a.shape, mybir.dt.from_np(a.dtype), kind="ExternalInput").ap()

    w1 = np.asarray(inputs["W_top1"])
    row = np.zeros((F, F), np.int64)
    row[np.triu_indices(F, k=1)] = np.arange(F * (F - 1) // 2)
    order = [row[min(f, (f + k) % F), max(f, (f + k) % F)] for f in range(F) for k in range(1, KOFF + 1)]
    emb_rows, pairs = F * D, F * (F - 1) // 2
    args = [
        dram("ids_dram", np.asarray(inputs["ids"]).view(np.uint32)),
        [dram(f"tbl_{f}_dram", inputs[f"tbl_{f}"]) for f in range(F)],
        dram("w1_emb_dram", w1[:emb_rows]),
        dram("w1_int_dram", w1[emb_rows:emb_rows + pairs][order]),
        dram("w1_dense_dram", w1[emb_rows + pairs:]),
        dram("b1_dram", np.asarray(inputs["b_top1"]).reshape(1, H1)),
        dram("w2_dram", inputs["W_top2"]),
        dram("b2_dram", np.asarray(inputs["b_top2"]).reshape(H2 // P, P).T),
        dram("w3_dram", np.asarray(inputs["W_top3"]).reshape(H2 // P, P).T),
        dram("dense_t_dram", np.asarray(inputs["dense_ctx"]).T),
        nc.dram_tensor("scratch_dram", (P, FX * QUAD), mybir.dt.float32, kind="Internal").ap(),
    ]
    out = nc.dram_tensor("out_dram", (B, 1), mybir.dt.float32, kind="ExternalOutput").ap()
    build(nc, *args, out.rearrange("b o -> o b"))
    r = run(nc, [arrays], core_ids=[0])
    return r.results[0]["out_dram"]
```

```python
import concourse.bass as bass
from concourse import mybir
from contextlib import ExitStack

P = 128
B, F, D = 512, 27, 128
NDENSE = 16
H1, H2 = 512, 256
T = B // P
GF = 3
G = F // GF
ROW_SLOTS = 6
TR_BANKS = 2
EMB_SLOTS = 3
SPLIT_SLOTS = 6
N = T * G
PUT_OFF = (0, G, 2 * G, 3 * G, 3 * G + 4)
BLOCKS = ((0, 11), (11, 18), (18, 23), (23, 27))
NZ = len(BLOCKS)
AUX = 1 + NDENSE
ROW0 = (0, 0, 0, AUX)
NW = F + NZ
QUAD = 32
HALF = QUAD // 2
ETI = P * F + QUAD - F
assert all(e * (e - a) + r <= P for (a, e), r in zip(BLOCKS, ROW0))


def groups_summed(n):
    return n + 1 - sum(p <= n for p in PUT_OFF)


def build(nc, ids, tables, w1_emb, w1_rest, w2, b2, w3, dense_t, scratch, out):
    fp32, fp32r, u32 = mybir.dt.float32, mybir.dt.float32r, mybir.dt.uint32
    ACT = mybir.ActivationFunctionType
    ALU = mybir.AluOpType
    ctx = ExitStack()
    with ctx:
        def sb(name, shape, dt=fp32):
            return ctx.enter_context(nc.sbuf_tensor(name, shape, dt))

        def bank(name):
            return ctx.enter_context(nc.psum_tensor(name, [P, 512], fp32))

        def sem(name):
            return ctx.enter_context(nc.semaphore(name))

        idx = sb("idx", [P, T, F], u32)
        ident = sb("ident", [P, P])
        rows = sb("rows", [P, ROW_SLOTS, GF, D])
        emb = sb("emb", [P, EMB_SLOTS, GF, P])
        emb_hi = sb("emb_hi", [P, SPLIT_SLOTS, GF, P], fp32r)
        emb_lo = sb("emb_lo", [P, SPLIT_SLOTS, GF, P], fp32r)
        emb_bf = sb("emb_bf", [P, ETI])
        w_hi = sb("w_hi", [P, NW, H1], fp32r)
        w_lo = sb("w_lo", [P, NW, H1], fp32r)
        w_raw = sb("w_raw", [P, 2, GF * H1])
        dots = w_raw[:, 0, 0:F * QUAD].rearrange("p (g i) -> p g i", g=F)
        h1 = w_raw[:, 1, 0:H1]
        z = sb("z", [P, NZ, P])
        z_hi = sb("z_hi", [P, NZ, P], fp32r)
        z_lo = sb("z_lo", [P, NZ, P], fp32r)
        w2_sb = sb("w2_sb", [P, H1 // P, H2])
        b2_sb = sb("b2_sb", [P, H2 // P])
        w3_sb = sb("w3_sb", [P, H2 // P])
        h1_t = sb("h1_t", [P, H1 // P, P])
        h2_t = sb("h2_t", [P, H2 // P, P])
        y = sb("y", [1, B])

        tr_ps = [bank(f"tr_ps{i}") for i in range(TR_BANKS)]
        dot_ps = [bank(f"dot_ps{i}") for i in range(2)]
        h1_ps = [bank(f"h1_ps{i}") for i in range(2)]
        h1t_ps = bank("h1t_ps")
        h2_ps = bank("h2_ps")

        ids_loaded = sem("ids_loaded")
        const_loaded = sem("const_loaded")
        ident_zeroed = sem("ident_zeroed")
        ident_ready = sem("ident_ready")
        pads_ready = sem("pads_ready")
        z_zeroed = sem("z_zeroed")
        gathered = [sem(f"gathered{i}") for i in range(ROW_SLOTS)]
        transposed = sem("transposed")
        emb_ready = sem("emb_ready")
        emb_bf_ready = sem("emb_bf_ready")
        hi_ready = sem("hi_ready")
        split_ready = sem("split_ready")
        group_summed = sem("group_summed")
        w_loaded = [sem(f"w_loaded{i}") for i in range(2)]
        w_hi_ready = sem("w_hi_ready")
        w_lo_ready = sem("w_lo_ready")
        dots_done = sem("dots_done")
        dots_copied = sem("dots_copied")
        dots_stored = [sem(f"dots_stored{r}") for r in range(NZ)]
        dense_loaded = sem("dense_loaded")
        z_loaded = [sem(f"z_loaded{h}") for h in range(2)]
        z_hi_ready = sem("z_hi_ready")
        z_ready = sem("z_ready")
        h1_done = sem("h1_done")
        h1_ready = sem("h1_ready")
        h1t_done = sem("h1t_done")
        h1t_ready = sem("h1t_ready")
        h2_done = sem("h2_done")
        h2_ready = sem("h2_ready")
        y_done = sem("y_done")
        y_ready = sem("y_ready")
        out_stored = sem("out_stored")

        block = ctx.enter_context(nc.Block())

        W_LOADS = G + 2

        def w_tiles(n):
            return slice(n * GF, (n + 1) * GF) if n < G else slice(F + 2 * (n - G), F + 2 * (n - G) + 2)

        @block.sync
        def _(sp):
            sp.dma_start(idx[:], ids.rearrange("(t p) f -> p t f", p=P)).then_inc(ids_loaded, 16)

            def load_w(n):
                if n >= 2:
                    sp.wait_ge(w_hi_ready, n - 1)
                    sp.wait_ge(w_lo_ready, n - 1)
                c = GF if n < G else 2
                src = w1_emb[n * GF * D:(n + 1) * GF * D, :] if n < G else w1_rest[2 * (n - G) * P:2 * (n - G + 1) * P, :]
                sp.dma_start(w_raw[:, n % 2, 0:c * H1].rearrange("k (f n) -> k f n", f=c),
                             src.rearrange("(f k) n -> k f n", f=c)).then_inc(w_loaded[n % 2], 16)

            load_w(0)
            load_w(1)
            sp.dma_start(w2_sb[:], w2.rearrange("(c k) n -> k c n", c=H1 // P)).then_inc(const_loaded, 16)
            with nc.allow_non_contiguous_dma(reason="256 biases and 256 weights onto partitions"):
                sp.dma_start(b2_sb[:], b2).then_inc(const_loaded, 16)
                sp.dma_start(w3_sb[:], w3).then_inc(const_loaded, 16)
            for n in range(2, W_LOADS):
                load_w(n)
            sp.wait_ge(z_zeroed, 2)
            for t in range(T):
                if t > 0:
                    sp.wait_ge(z_ready, 2 * t)
                sp.dma_start(z[1:AUX, NZ - 1, :], dense_t[:, t * P:(t + 1) * P]).then_inc(dense_loaded, 16)
                sp.wait_ge(dots_copied, 2 * (t + 1))
                if t > 0:
                    for h in range(2):
                        sp.wait_ge(z_loaded[h], 32 * t)
                for r, (a, e) in enumerate(BLOCKS):
                    sp.dma_start(scratch[r], dots[:, a:e, :].rearrange("p g i -> p (g i)")).then_inc(dots_stored[r], 16)
                for r, (a, e) in enumerate(BLOCKS):
                    sp.wait_ge(dots_stored[r], 16 * (t + 1))
                    pairs, w = e * (e - a), (e - a) * QUAD
                    src = bass.AP(tensor=scratch[r].tensor, offset=0, ap=[[QUAD, pairs], [QUAD * w, 4], [1, QUAD]])
                    sp.dma_start(z[ROW0[r]:ROW0[r] + pairs, r, :].rearrange("p (j i) -> p j i", j=4),
                                 src).then_inc(z_loaded[r // 2], 16)
            sp.wait_ge(y_ready, T)
            sp.dma_start(out, y[:]).then_inc(out_stored, 16)
            sp.wait_ge(out_stored, 16)

        @block.gpsimd
        def _(pool):
            nc.gpsimd.memset(ident[:], 0.0).then_inc(ident_zeroed, 1)
            pool.wait_ge(ident_zeroed, 1)
            nc.gpsimd.affine_select(out=ident[:], in_=ident[:], compare_op=ALU.not_equal, fill=1.0, base=0,
                                    pattern=[[-1, P]], channel_multiplier=1).then_inc(ident_ready, 1)
            pool.wait_ge(ids_loaded, 16)
            for t in range(T):
                for g in range(G):
                    n = t * G + g
                    if n >= ROW_SLOTS:
                        pool.wait_ge(transposed, n - ROW_SLOTS + 1)
                    for c in range(GF):
                        f = g * GF + c
                        nc.gpsimd.indirect_dma_start(
                            out=rows[:, n % ROW_SLOTS, c, :], out_offset=None, in_=tables[f][:, :],
                            in_offset=bass.IndirectOffsetOnAxis(ap=idx[:, t, f:f + 1], axis=0),
                        ).then_inc(gathered[n % ROW_SLOTS], 16)

        @block.scalar
        def _(act):
            def sample_major(t, g):
                n = t * G + g
                act.wait_ge(emb_ready, n + 1)
                if g == 0 and t > 0:
                    act.wait_ge(dots_done, 2 * t)
                dst = emb_bf[:, 0:P * F].rearrange("p (b f) -> p b f", f=F)[:, :, g * GF:(g + 1) * GF]
                nc.scalar.activation(dst, emb[:, n % EMB_SLOTS, :, :].rearrange("p f b -> p b f"),
                                     ACT.Copy).then_inc(emb_bf_ready, 1)

            def split_w_hi(n):
                act.wait_ge(w_loaded[n % 2], 16 * (n // 2 + 1))
                c = GF if n < G else 2
                nc.scalar.activation(w_hi[:, w_tiles(n), :].rearrange("k f n -> k (f n)"),
                                     w_raw[:, n % 2, 0:c * H1], ACT.Copy).then_inc(w_hi_ready, 1)

            def finish_h1(t):
                act.wait_ge(h1_done, 2 * (t + 1))
                if t > 0:
                    act.wait_ge(h1t_done, t)
                nc.scalar.activation(h1, h1_ps[t % 2][:], ACT.Relu).then_inc(h1_ready, 1)

            def finish_h2(t):
                act.wait_ge(h2_done, t + 1)
                if t > 0:
                    act.wait_ge(y_done, t)
                if t == 0:
                    act.wait_ge(const_loaded, 48)
                for m in range(H2 // P):
                    nc.scalar.activation(h2_t[:, m, :], h2_ps[:, m * P:(m + 1) * P], ACT.Relu,
                                         bias=b2_sb[:, m:m + 1]).then_inc(h2_ready, 1)

            split_w_hi(0)
            split_w_hi(1)
            for t in range(T):
                for g in range(G):
                    n = t * G + g
                    act.wait_ge(transposed, n + 1)
                    if n >= EMB_SLOTS:
                        act.wait_ge(split_ready, n - EMB_SLOTS + 1)
                        act.wait_ge(emb_bf_ready, n - EMB_SLOTS + 1)
                    nc.scalar.activation(emb[:, n % EMB_SLOTS, :, :].rearrange("p f b -> p (f b)"),
                                         tr_ps[n % TR_BANKS][:, 0:GF * P], ACT.Copy).then_inc(emb_ready, 1)
                    if g > 0:
                        sample_major(t, g - 1)
                    if n + 2 < W_LOADS:
                        split_w_hi(n + 2)
                    if g == G - 1:
                        sample_major(t, g)
                    if t > 0 and g == 5:
                        finish_h1(t - 1)
                    if t > 0 and g == 7:
                        finish_h2(t - 1)
            finish_h1(T - 1)
            finish_h2(T - 1)

        @block.vector
        def _(dve):
            nc.vector.memset(z[:], 0.0).then_inc(z_zeroed, 1)
            dve.wait_ge(z_zeroed, 1)
            nc.vector.memset(z[0:1, NZ - 1, :], 1.0).then_inc(z_zeroed, 1)
            nc.vector.memset(emb_bf[:, P * F:ETI], 0.0).then_inc(pads_ready, 1)

            def split(t, g):
                n = t * G + g
                dve.wait_ge(emb_ready, n + 1)
                if n >= SPLIT_SLOTS:
                    dve.wait_ge(group_summed, n - SPLIT_SLOTS + 1)
                nc.vector.tensor_copy(emb_hi[:, n % SPLIT_SLOTS, :, :], emb[:, n % EMB_SLOTS, :, :]).then_inc(hi_ready, 1)
                dve.wait_ge(hi_ready, n + 1)
                nc.vector.tensor_tensor(emb_lo[:, n % SPLIT_SLOTS, :, :], emb[:, n % EMB_SLOTS, :, :], emb_hi[:, n % SPLIT_SLOTS, :, :].bitcast(fp32),
                                        ALU.subtract).then_inc(split_ready, 1)

            def split_w_lo(n):
                dve.wait_ge(w_hi_ready, n + 1)
                c, tiles = GF if n < G else 2, w_tiles(n)
                nc.vector.tensor_tensor(w_lo[:, tiles, :].rearrange("k f n -> k (f n)"), w_raw[:, n % 2, 0:c * H1],
                                        w_hi[:, tiles, :].rearrange("k f n -> k (f n)").bitcast(fp32),
                                        ALU.subtract).then_inc(w_lo_ready, 1)

            def copy_dots(t):
                if t == 0:
                    dve.wait_ge(w_lo_ready, W_LOADS)
                else:
                    for r in range(NZ):
                        dve.wait_ge(dots_stored[r], 16 * t)
                for h in range(2):
                    dve.wait_ge(dots_done, 2 * t + h + 1)
                    nc.vector.tensor_copy(
                        dots[:, :, h * HALF:(h + 1) * HALF],
                        dot_ps[h][:, 0:HALF * F].rearrange("p (i g) -> p g i", g=F)).then_inc(dots_copied, 1)

            def split_z(t, h):
                dve.wait_ge(z_loaded[h], 32 * (t + 1))
                if h == 1:
                    dve.wait_ge(dense_loaded, 16 * (t + 1))
                if t > 0:
                    dve.wait_ge(h1_done, 2 * t)
                v = slice(2 * h, 2 * h + 2)
                nc.vector.tensor_copy(z_hi[:, v, :], z[:, v, :]).then_inc(z_hi_ready, 1)
                dve.wait_ge(z_hi_ready, 2 * t + h + 1)
                nc.vector.tensor_tensor(z_lo[:, v, :], z[:, v, :], z_hi[:, v, :].bitcast(fp32),
                                        ALU.subtract).then_inc(z_ready, 1)

            def copy_h1t(t):
                dve.wait_ge(h1t_done, t + 1)
                if t > 0:
                    dve.wait_ge(h2_done, t)
                nc.vector.tensor_copy(h1_t[:].rearrange("p c b -> p (c b)"), h1t_ps[:]).then_inc(h1t_ready, 1)

            def copy_y(t):
                dve.wait_ge(y_done, t + 1)
                nc.vector.tensor_copy(y[0:1, t * P:(t + 1) * P], h2_ps[0:1, H2:H2 + P]).then_inc(y_ready, 1)

            split_w_lo(0)
            split_w_lo(1)
            for t in range(T):
                for g in range(G):
                    split(t, g)
                    if t * G + g + 2 < W_LOADS:
                        split_w_lo(t * G + g + 2)
                    if t > 0:
                        if g == 0:
                            copy_dots(t - 1)
                        if g == 4:
                            split_z(t - 1, 0)
                            split_z(t - 1, 1)
                        if g == 6:
                            copy_h1t(t - 1)
                        if g == 8:
                            copy_y(t - 1)
            copy_dots(T - 1)
            split_z(T - 1, 0)
            split_z(T - 1, 1)
            copy_h1t(T - 1)
            copy_y(T - 1)

        @block.tensor
        def _(pe):
            def transpose_group(t, g):
                n = t * G + g
                pe.wait_ge(gathered[n % ROW_SLOTS], 16 * GF * (n // ROW_SLOTS + 1))
                if n >= TR_BANKS:
                    pe.wait_ge(emb_ready, n - TR_BANKS + 1)
                for c in range(GF):
                    last = nc.tensor.transpose(tr_ps[n % TR_BANKS][:, c * P:(c + 1) * P], rows[:, n % ROW_SLOTS, c, :], ident[:])
                last.then_inc(transposed, 1)

            def product(t, m, hi, lo, w, start, stop):
                return nc.tensor.matmul(h1_ps[t % 2][:], lo if m == 2 else hi, (w_lo if m == 1 else w_hi)[:, w, :],
                                        start=start and m == 0, stop=stop and m == 2)

            def sum_group(n):
                t, g = divmod(n, G)
                pe.wait_ge(split_ready, n + 1)
                if t == 0:
                    pe.wait_ge(w_lo_ready, g + 1)
                if g == 0 and t > 1:
                    pe.wait_ge(h1_ready, t - 1)
                for c in range(GF):
                    for m in range(3):
                        last = product(t, m, emb_hi[:, n % SPLIT_SLOTS, c, :], emb_lo[:, n % SPLIT_SLOTS, c, :],
                                       g * GF + c, g == 0 and c == 0, False)
                last.then_inc(group_summed, 1)

            def interact(t, h):
                if h == 0:
                    pe.wait_ge(emb_bf_ready, G * (t + 1))
                if t > 0:
                    pe.wait_ge(dots_copied, 2 * (t - 1) + h + 1)
                for i in range(HALF):
                    for j in range(4):
                        b = (QUAD * j + h * HALF + i) * F
                        last = nc.tensor.matmul(dot_ps[h][QUAD * j:QUAD * (j + 1), i * F:(i + 1) * F],
                                                emb_bf[:, b:b + QUAD], emb_bf[:, b:b + F], start=True, stop=True)
                last.then_inc(dots_done, 1)

            def sum_pairs_and_dense(t):
                if t == 0:
                    pe.wait_ge(w_lo_ready, W_LOADS)
                for h in range(2):
                    pe.wait_ge(z_ready, 2 * t + h + 1)
                    for r in (2 * h, 2 * h + 1):
                        for m in range(3):
                            last = product(t, m, z_hi[:, r, :], z_lo[:, r, :], F + r, False, r == NZ - 1)
                    last.then_inc(h1_done, 1)

            def transpose_h1(t):
                pe.wait_ge(h1_ready, t + 1)
                if t > 0:
                    pe.wait_ge(h1t_ready, t)
                for c in range(H1 // P):
                    last = nc.tensor.transpose(h1t_ps[:, c * P:(c + 1) * P], h1[:, c * P:(c + 1) * P], ident[:])
                last.then_inc(h1t_done, 1)

            def second_layer(t):
                pe.wait_ge(h1t_ready, t + 1)
                if t == 0:
                    pe.wait_ge(const_loaded, 48)
                else:
                    pe.wait_ge(y_ready, t)
                for m in range(H2 // P):
                    for c in range(H1 // P):
                        last = nc.tensor.matmul(h2_ps[:, m * P:(m + 1) * P], w2_sb[:, c, m * P:(m + 1) * P],
                                                h1_t[:, c, :], start=c == 0, stop=c == H1 // P - 1)
                last.then_inc(h2_done, 1)

            def third_layer(t):
                pe.wait_ge(h2_ready, (H2 // P) * (t + 1))
                for m in range(H2 // P):
                    last = nc.tensor.matmul(h2_ps[0:1, H2:H2 + P], w3_sb[:, m:m + 1], h2_t[:, m, :],
                                            start=m == 0, stop=m == H2 // P - 1)
                last.then_inc(y_done, 1)

            pe.wait_ge(ident_ready, 1)
            summed = 0
            for t in range(T):
                for g in range(G):
                    transpose_group(t, g)
                    if t > 0 and g == 0:
                        if t == 1:
                            pe.wait_ge(pads_ready, 1)
                        interact(t - 1, 0)
                        sum_group(summed)
                        summed += 1
                        interact(t - 1, 1)
                    for n in range(summed, groups_summed(t * G + g)):
                        sum_group(n)
                        summed = n + 1
                    if t > 0:
                        if g == 5:
                            sum_pairs_and_dense(t - 1)
                        if g == 6:
                            transpose_h1(t - 1)
                        if g == 7:
                            second_layer(t - 1)
                        if g == 8:
                            third_layer(t - 1)
            interact(T - 1, 0)
            sum_group(summed)
            interact(T - 1, 1)
            for n in range(summed + 1, N):
                sum_group(n)
            sum_pairs_and_dense(T - 1)
            transpose_h1(T - 1)
            second_layer(T - 1)
            third_layer(T - 1)


def kernel(**inputs):
    import numpy as np
    import concourse.bacc as bacc
    from concourse.bass_utils import run_bass_kernel_spmd as run

    nc = bacc.Bacc("TRN2", target_bir_lowering=False, num_devices=1)
    arrays = {}

    def dram(name, a):
        arrays[name] = a = np.ascontiguousarray(a)
        return nc.dram_tensor(name, a.shape, mybir.dt.from_np(a.dtype), kind="ExternalInput").ap()

    w1 = np.asarray(inputs["W_top1"])
    emb_rows, pairs = F * D, F * (F - 1) // 2
    pair_row = np.full((F, F), -1)
    pair_row[np.triu_indices(F, k=1)] = np.arange(pairs)
    rest = np.full((NZ, P), -1)
    for r, (a, e) in enumerate(BLOCKS):
        rest[r, ROW0[r]:ROW0[r] + e * (e - a)] = pair_row[:e, a:e].reshape(-1)
    rest[NZ - 1, 1:AUX] = pairs + np.arange(NDENSE)
    rest[NZ - 1, 0] = pairs + NDENSE
    below = np.concatenate([w1[emb_rows:], np.asarray(inputs["b_top1"])[None, :], np.zeros((1, H1), w1.dtype)])
    args = [
        dram("ids_dram", np.asarray(inputs["ids"]).view(np.uint32)),
        [dram(f"tbl_{f}_dram", inputs[f"tbl_{f}"]) for f in range(F)],
        dram("w1_emb_dram", w1[:emb_rows]),
        dram("w1_rest_dram", below[rest.reshape(-1)]),
        dram("w2_dram", inputs["W_top2"]),
        dram("b2_dram", np.asarray(inputs["b_top2"]).reshape(H2 // P, P).T),
        dram("w3_dram", np.asarray(inputs["W_top3"]).reshape(H2 // P, P).T),
        dram("dense_t_dram", np.asarray(inputs["dense_ctx"]).T),
        [nc.dram_tensor(f"scratch{r}_dram", (P, (e - a) * QUAD), mybir.dt.float32, kind="Internal").ap()
         for r, (a, e) in enumerate(BLOCKS)],
    ]
    out = nc.dram_tensor("out_dram", (B, 1), mybir.dt.float32, kind="ExternalOutput").ap()
    build(nc, *args, out.rearrange("b o -> o b"))
    r = run(nc, [arrays], core_ids=[0])
    return r.results[0]["out_dram"]
```

```python
import concourse.bass as bass
from concourse import mybir
from contextlib import ExitStack

P = 128
B, F, D = 512, 27, 128
NDENSE = 16
H1, H2 = 512, 256
T = B // P
GF = 3
G = F // GF
ROW_SLOTS = 6
TR_BANKS = 3
EMB_SLOTS = 3
W_SLOTS = 6
W_AHEAD = 5
SPLIT_SLOTS = 6
N = T * G
PUT_OFF = (0, 0, 0, 1, 1, G, 2 * G, 2 * G, 3 * G, 3 * G, N - 1)
BETWEEN = (3, 3, 3, 0)
BLOCKS = ((0, 11), (11, 18), (18, 23), (23, 27))
NZ = len(BLOCKS)
AUX = 1 + NDENSE
ROW0 = (0, 0, 0, AUX)
NW = F + NZ
NA = NW + 2
QUAD = 32
HALF = QUAD // 2
ETI = P * F + QUAD - F
assert all(e * (e - a) + r <= P for (a, e), r in zip(BLOCKS, ROW0))


def features_summed(n):
    return GF * (n + 1) - sum(p <= n for p in PUT_OFF)


def build(nc, ids, tables, w1_emb, w1_rest, w2, b2, w3, dense_t, scratch, out):
    fp32, fp32r, u32 = mybir.dt.float32, mybir.dt.float32r, mybir.dt.uint32
    ACT = mybir.ActivationFunctionType
    ALU = mybir.AluOpType
    ctx = ExitStack()
    with ctx:
        def sb(name, shape, dt=fp32):
            return ctx.enter_context(nc.sbuf_tensor(name, shape, dt))

        def bank(name):
            return ctx.enter_context(nc.psum_tensor(name, [P, 512], fp32))

        def sem(name):
            return ctx.enter_context(nc.semaphore(name))

        idx = sb("idx", [P, T, F], u32)
        ident = sb("ident", [P, P])
        rows = sb("rows", [P, ROW_SLOTS, GF, D])
        emb = sb("emb", [P, EMB_SLOTS, GF, P])
        emb_hi = sb("emb_hi", [P, SPLIT_SLOTS, GF, P], fp32r)
        emb_lo = sb("emb_lo", [P, SPLIT_SLOTS, GF, P], fp32r)
        emb_sm = sb("emb_sm", [P, ETI])
        w_hi = sb("w_hi", [P, NA, H1], fp32r)
        w_lo = sb("w_lo", [P, NA, H1], fp32r)
        w_raw = sb("w_raw", [P, W_SLOTS, H1])
        dots = sb("dots", [P, F, QUAD])
        h1 = w_raw[:, 0, :]
        z = sb("z", [P, NZ, P])
        z_hi = sb("z_hi", [P, NZ, P], fp32r)
        z_lo = sb("z_lo", [P, NZ, P], fp32r)
        b2_sb = sb("b2_sb", [P, H2])
        w3_sb = sb("w3_sb", [P, H2])
        h1t_hi = sb("h1t_hi", [P, H1 // P, P], fp32r)
        h1t_lo = sb("h1t_lo", [P, H1 // P, P], fp32r)
        h2 = sb("h2", [P, H2])
        y = sb("y", [P, T])

        tr_ps = [bank(f"tr_ps{i}") for i in range(TR_BANKS)]
        dot_ps = [bank(f"dot_ps{i}") for i in range(2)]
        h1_ps = [bank(f"h1_ps{i}") for i in range(2)]
        h2_ps = bank("h2_ps")

        ids_loaded = sem("ids_loaded")
        const_loaded = sem("const_loaded")
        ident_zeroed = sem("ident_zeroed")
        ident_ready = sem("ident_ready")
        pads_ready = sem("pads_ready")
        z_zeroed = sem("z_zeroed")
        gathered = [sem(f"gathered{i}") for i in range(ROW_SLOTS)]
        transposed = sem("transposed")
        emb_ready = sem("emb_ready")
        emb_sm_ready = sem("emb_sm_ready")
        hi_ready = sem("hi_ready")
        split_ready = sem("split_ready")
        feature_summed = sem("feature_summed")
        w_loaded = [sem(f"w_loaded{i}") for i in range(W_SLOTS)]
        w_hi_ready = sem("w_hi_ready")
        w_lo_ready = sem("w_lo_ready")
        dots_done = sem("dots_done")
        dots_copied = sem("dots_copied")
        dots_stored = [sem(f"dots_stored{r}") for r in range(NZ)]
        dense_loaded = sem("dense_loaded")
        z_loaded = [sem(f"z_loaded{h}") for h in range(2)]
        z_hi_ready = sem("z_hi_ready")
        z_ready = sem("z_ready")
        h1_done = sem("h1_done")
        h1_ready = sem("h1_ready")
        h1t_done = sem("h1t_done")
        h1t_hi_ready = sem("h1t_hi_ready")
        h1t_ready = sem("h1t_ready")
        h2_done = sem("h2_done")
        h2_out = sem("h2_out")
        y_ready = sem("y_ready")
        out_stored = sem("out_stored")

        block = ctx.enter_context(nc.Block())

        def w_turn(n):
            return range(0, W_AHEAD) if n < 0 else range(W_AHEAD + 3 * n, min(W_AHEAD + 3 * n + 3, NA))

        @block.sync
        def _(sp):
            sp.dma_start(idx[:], ids.rearrange("(t p) f -> p t f", p=P)).then_inc(ids_loaded, 16)

            def load_w(n):
                if n >= W_SLOTS:
                    sp.wait_ge(w_lo_ready, n - W_SLOTS + 1)
                if n < F:
                    dst, src = w_raw[:, n % W_SLOTS, :], w1_emb[n * D:(n + 1) * D, :]
                elif n < NW:
                    dst, src = w_raw[:, n % W_SLOTS, :], w1_rest[(n - F) * P:(n - F + 1) * P, :]
                else:
                    dst = w_raw[:, n % W_SLOTS, :].rearrange("p (c n) -> p c n", c=2)
                    src = w2[(n - NW) * 2 * P:(n - NW + 1) * 2 * P, :].rearrange("(c k) n -> k c n", c=2)
                sp.dma_start(dst, src).then_inc(w_loaded[n % W_SLOTS], 16)

            for n in range(NA):
                load_w(n)
            sp.dma_start(b2_sb[:], b2.partition_broadcast(P)).then_inc(const_loaded, 16)
            sp.dma_start(w3_sb[:], w3.partition_broadcast(P)).then_inc(const_loaded, 16)
            sp.wait_ge(z_zeroed, 2)
            for t in range(T):
                if t > 0:
                    sp.wait_ge(z_ready, 2 * t)
                sp.dma_start(z[1:AUX, NZ - 1, :], dense_t[:, t * P:(t + 1) * P]).then_inc(dense_loaded, 16)
                sp.wait_ge(dots_copied, 2 * (t + 1))
                if t > 0:
                    for h in range(2):
                        sp.wait_ge(z_loaded[h], 32 * t)
                for r, (a, e) in enumerate(BLOCKS):
                    sp.dma_start(scratch[r], dots[:, a:e, :].rearrange("p g i -> p (g i)")).then_inc(dots_stored[r], 16)
                for r, (a, e) in enumerate(BLOCKS):
                    sp.wait_ge(dots_stored[r], 16 * (t + 1))
                    pairs, w = e * (e - a), (e - a) * QUAD
                    src = bass.AP(tensor=scratch[r].tensor, offset=0, ap=[[QUAD, pairs], [QUAD * w, 4], [1, QUAD]])
                    sp.dma_start(z[ROW0[r]:ROW0[r] + pairs, r, :].rearrange("p (j i) -> p j i", j=4),
                                 src).then_inc(z_loaded[r // 2], 16)
            sp.wait_ge(y_ready, T)
            with nc.allow_non_contiguous_dma(reason="512 results, one at a time"):
                sp.dma_start(out, y[:]).then_inc(out_stored, 16)
            sp.wait_ge(out_stored, 16)

        @block.gpsimd
        def _(pool):
            nc.gpsimd.memset(ident[:], 0.0).then_inc(ident_zeroed, 1)
            pool.wait_ge(ident_zeroed, 1)
            nc.gpsimd.affine_select(out=ident[:], in_=ident[:], compare_op=ALU.not_equal, fill=1.0, base=0,
                                    pattern=[[-1, P]], channel_multiplier=1).then_inc(ident_ready, 1)
            pool.wait_ge(ids_loaded, 16)
            for t in range(T):
                for g in range(G):
                    n = t * G + g
                    if n >= ROW_SLOTS:
                        pool.wait_ge(transposed, n - ROW_SLOTS + 1)
                    for c in range(GF):
                        f = g * GF + c
                        nc.gpsimd.indirect_dma_start(
                            out=rows[:, n % ROW_SLOTS, c, :], out_offset=None, in_=tables[f][:, :],
                            in_offset=bass.IndirectOffsetOnAxis(ap=idx[:, t, f:f + 1], axis=0),
                        ).then_inc(gathered[n % ROW_SLOTS], 16)

        @block.scalar
        def _(act):
            def sample_major(t, g):
                n = t * G + g
                act.wait_ge(emb_ready, n + 1)
                if g == 0 and t > 0:
                    act.wait_ge(dots_done, 2 * t)
                dst = emb_sm[:, 0:P * F].rearrange("p (b f) -> p b f", f=F)[:, :, g * GF:(g + 1) * GF]
                nc.scalar.activation(dst, emb[:, n % EMB_SLOTS, :, :].rearrange("p f b -> p b f"),
                                     ACT.Copy).then_inc(emb_sm_ready, 1)

            def split_w_hi(n):
                act.wait_ge(w_loaded[n % W_SLOTS], 16 * (n // W_SLOTS + 1))
                nc.scalar.activation(w_hi[:, n, :], w_raw[:, n % W_SLOTS, :], ACT.Copy).then_inc(w_hi_ready, 1)

            def finish_h1(t):
                act.wait_ge(h1_done, 2 * (t + 1))
                if t > 0:
                    act.wait_ge(h1t_done, 2 * t)
                for h in range(2):
                    v = slice(h * H1 // 2, (h + 1) * H1 // 2)
                    nc.scalar.activation(h1[:, v], h1_ps[t % 2][:, v], ACT.Relu).then_inc(h1_ready, 1)

            def split_h1t_hi(t):
                if t > 0:
                    act.wait_ge(h2_done, t)
                for h in range(2):
                    act.wait_ge(h1t_done, 2 * t + h + 1)
                    nc.scalar.activation(h1t_hi[:, 2 * h:2 * h + 2, :].rearrange("p c b -> p (c b)"),
                                         dot_ps[h][:, 0:H1 // 2], ACT.Copy).then_inc(h1t_hi_ready, 1)

            for w in w_turn(-1):
                split_w_hi(w)
            for t in range(T):
                for g in range(G):
                    n = t * G + g
                    act.wait_ge(transposed, n + 1)
                    if n >= EMB_SLOTS:
                        act.wait_ge(split_ready, n - EMB_SLOTS + 1)
                        act.wait_ge(emb_sm_ready, n - EMB_SLOTS + 1)
                    nc.scalar.activation(emb[:, n % EMB_SLOTS, :, :].rearrange("p f b -> p (f b)"),
                                         tr_ps[n % TR_BANKS][:, 0:GF * P], ACT.Copy).then_inc(emb_ready, 1)
                    if 0 < g < G - 1:
                        sample_major(t, g - 1)
                    if g == G - 1:
                        sample_major(t, g)
                    for w in w_turn(n):
                        split_w_hi(w)
                    if g == G - 2:
                        sample_major(t, g)
                    if t > 0 and g == 5:
                        finish_h1(t - 1)
                    if t > 0 and g == 6:
                        split_h1t_hi(t - 1)
            finish_h1(T - 1)
            split_h1t_hi(T - 1)

        @block.vector
        def _(dve):
            nc.vector.memset(z[:], 0.0).then_inc(z_zeroed, 1)
            dve.wait_ge(z_zeroed, 1)
            nc.vector.memset(z[0:1, NZ - 1, :], 1.0).then_inc(z_zeroed, 1)
            nc.vector.memset(emb_sm[:, P * F:ETI], 0.0).then_inc(pads_ready, 1)

            def split(t, g):
                n = t * G + g
                dve.wait_ge(emb_ready, n + 1)
                if n >= SPLIT_SLOTS:
                    dve.wait_ge(feature_summed, GF * (n - SPLIT_SLOTS + 1))
                nc.vector.tensor_copy(emb_hi[:, n % SPLIT_SLOTS, :, :], emb[:, n % EMB_SLOTS, :, :]).then_inc(hi_ready, 1)
                dve.wait_ge(hi_ready, n + 1)
                nc.vector.tensor_tensor(emb_lo[:, n % SPLIT_SLOTS, :, :], emb[:, n % EMB_SLOTS, :, :], emb_hi[:, n % SPLIT_SLOTS, :, :].bitcast(fp32),
                                        ALU.subtract).then_inc(split_ready, 1)

            def split_w_lo(n):
                dve.wait_ge(w_hi_ready, n + 1)
                nc.vector.tensor_tensor(w_lo[:, n, :], w_raw[:, n % W_SLOTS, :], w_hi[:, n, :].bitcast(fp32),
                                        ALU.subtract).then_inc(w_lo_ready, 1)

            def copy_dots(t):
                if t > 0:
                    for r in range(NZ):
                        dve.wait_ge(dots_stored[r], 16 * t)
                for h in range(2):
                    dve.wait_ge(dots_done, 2 * t + h + 1)
                    nc.vector.tensor_copy(
                        dots[:, :, h * HALF:(h + 1) * HALF],
                        dot_ps[h][:, 0:HALF * F].rearrange("p (i g) -> p g i", g=F)).then_inc(dots_copied, 1)

            def split_z(t, h):
                dve.wait_ge(z_loaded[h], 32 * (t + 1))
                if h == 1:
                    dve.wait_ge(dense_loaded, 16 * (t + 1))
                if t > 0:
                    dve.wait_ge(h1_done, 2 * t)
                v = slice(2 * h, 2 * h + 2)
                nc.vector.tensor_copy(z_hi[:, v, :], z[:, v, :]).then_inc(z_hi_ready, 1)
                dve.wait_ge(z_hi_ready, 2 * t + h + 1)
                nc.vector.tensor_tensor(z_lo[:, v, :], z[:, v, :], z_hi[:, v, :].bitcast(fp32),
                                        ALU.subtract).then_inc(z_ready, 1)

            def split_h1t_lo(t):
                if t > 0:
                    dve.wait_ge(h2_done, t)
                for h in range(2):
                    hi = h1t_hi[:, 2 * h:2 * h + 2, :].rearrange("p c b -> p (c b)")
                    lo = h1t_lo[:, 2 * h:2 * h + 2, :].rearrange("p c b -> p (c b)")
                    dve.wait_ge(h1t_hi_ready, 2 * t + h + 1)
                    nc.vector.tensor_tensor(lo, dot_ps[h][:, 0:H1 // 2], hi.bitcast(fp32),
                                            ALU.subtract).then_inc(h1t_ready, 1)

            def finish(t):
                dve.wait_ge(h2_done, t + 1)
                if t == 0:
                    dve.wait_ge(const_loaded, 32)
                else:
                    dve.wait_ge(y_ready, t)
                nc.vector.tensor_tensor(h2[:], h2_ps[:, 0:H2], b2_sb[:], ALU.add).then_inc(h2_out, 1)
                dve.wait_ge(h2_out, t + 1)
                nc.vector.scalar_tensor_tensor(out=h2[:], in0=h2[:], scalar=0.0, in1=w3_sb[:], op0=ALU.max,
                                               op1=ALU.mult, accum_out=y[:, t:t + 1]).then_inc(y_ready, 1)

            for w in w_turn(-1):
                split_w_lo(w)
            for t in range(T):
                for g in range(G):
                    split(t, g)
                    for w in w_turn(t * G + g):
                        split_w_lo(w)
                    if t > 0:
                        if g == 4:
                            split_z(t - 1, 0)
                            split_z(t - 1, 1)
                        if g == 6:
                            split_h1t_lo(t - 1)
                        if g == 8:
                            finish(t - 1)
                    if g == G - 1:
                        copy_dots(t)
            split_z(T - 1, 0)
            split_z(T - 1, 1)
            split_h1t_lo(T - 1)
            finish(T - 1)

        @block.tensor
        def _(pe):
            def transpose_group(t, g):
                n = t * G + g
                pe.wait_ge(gathered[n % ROW_SLOTS], 16 * GF * (n // ROW_SLOTS + 1))
                if n >= TR_BANKS:
                    pe.wait_ge(emb_ready, n - TR_BANKS + 1)
                for c in range(GF):
                    last = nc.tensor.transpose(tr_ps[n % TR_BANKS][:, c * P:(c + 1) * P], rows[:, n % ROW_SLOTS, c, :], ident[:])
                last.then_inc(transposed, 1)

            def product(t, m, hi, lo, w, start, stop):
                return nc.tensor.matmul(h1_ps[t % 2][:], lo if m == 2 else hi, (w_lo if m == 1 else w_hi)[:, w, :],
                                        start=start and m == 0, stop=stop and m == 2)

            def sum_feature(k):
                n, c = divmod(k, GF)
                t, g = divmod(n, G)
                if c == 0:
                    pe.wait_ge(split_ready, n + 1)
                if t == 0:
                    pe.wait_ge(w_lo_ready, g * GF + c + 1)
                if g == 0 and c == 0 and t > 1:
                    pe.wait_ge(h1_ready, 2 * (t - 1))
                for m in range(3):
                    last = product(t, m, emb_hi[:, n % SPLIT_SLOTS, c, :], emb_lo[:, n % SPLIT_SLOTS, c, :],
                                   g * GF + c, g == 0 and c == 0, False)
                last.then_inc(feature_summed, 1)

            def interact(t, h):
                if h == 0:
                    pe.wait_ge(emb_sm_ready, G * (t + 1))
                if t > 0:
                    pe.wait_ge(dots_copied, 2 * (t - 1) + h + 1)
                    pe.wait_ge(h1t_ready, 2 * (t - 1) + h + 1)
                for i in range(HALF):
                    for j in range(4):
                        b = (QUAD * j + h * HALF + i) * F
                        last = nc.tensor.matmul(dot_ps[h][QUAD * j:QUAD * (j + 1), i * F:(i + 1) * F],
                                                emb_sm[:, b:b + QUAD], emb_sm[:, b:b + F], start=True, stop=True)
                last.then_inc(dots_done, 1)

            def sum_pairs_and_dense(t):
                if t == 0:
                    pe.wait_ge(w_lo_ready, NW)
                for h in range(2):
                    pe.wait_ge(z_ready, 2 * t + h + 1)
                    for r in (2 * h, 2 * h + 1):
                        for m in range(3):
                            last = product(t, m, z_hi[:, r, :], z_lo[:, r, :], F + r, False, r == NZ - 1)
                    last.then_inc(h1_done, 1)

            def transpose_h1(t):
                for h in range(2):
                    pe.wait_ge(h1_ready, 2 * t + h + 1)
                    for c in range(2):
                        q = 2 * h + c
                        last = nc.tensor.transpose(dot_ps[h][:, c * P:(c + 1) * P], h1[:, q * P:(q + 1) * P], ident[:])
                    last.then_inc(h1t_done, 1)

            def second_layer(t):
                if t == 0:
                    pe.wait_ge(w_lo_ready, NA)
                else:
                    pe.wait_ge(h2_out, t)
                def part(m, c):
                    v = slice(c % 2 * H2, (c % 2 + 1) * H2)
                    return nc.tensor.matmul(h2_ps[:, 0:H2], (h1t_lo if m == 2 else h1t_hi)[:, c, :],
                                            (w_lo if m == 1 else w_hi)[:, NW + c // 2, v],
                                            start=c == 0 and m == 0, stop=c == H1 // P - 1 and m == 2)

                for h in range(2):
                    pe.wait_ge(h1t_hi_ready, 2 * t + h + 1)
                    for c in (2 * h, 2 * h + 1):
                        part(0, c)
                        part(1, c)
                for h in range(2):
                    pe.wait_ge(h1t_ready, 2 * t + h + 1)
                    for c in (2 * h, 2 * h + 1):
                        last = part(2, c)
                last.then_inc(h2_done, 1)

            pe.wait_ge(ident_ready, 1)
            summed = 0
            for t in range(T):
                for g in range(G):
                    transpose_group(t, g)
                    for k in range(summed, features_summed(t * G + g)):
                        sum_feature(k)
                        summed = k + 1
                    if t > 0:
                        if g == 5:
                            sum_pairs_and_dense(t - 1)
                        if g == 6:
                            transpose_h1(t - 1)
                        if g == 7:
                            second_layer(t - 1)
                    if g == G - 1:
                        if t == 0:
                            pe.wait_ge(pads_ready, 1)
                        interact(t, 0)
                        for k in range(summed, summed + BETWEEN[t]):
                            sum_feature(k)
                            summed = k + 1
                        interact(t, 1)
            for k in range(summed, N * GF):
                sum_feature(k)
            sum_pairs_and_dense(T - 1)
            transpose_h1(T - 1)
            second_layer(T - 1)


def kernel(**inputs):
    import numpy as np
    import concourse.bacc as bacc
    from concourse.bass_utils import run_bass_kernel_spmd as run

    nc = bacc.Bacc("TRN2", target_bir_lowering=False, num_devices=1)
    arrays = {}

    def dram(name, a):
        arrays[name] = a = np.ascontiguousarray(a)
        return nc.dram_tensor(name, a.shape, mybir.dt.from_np(a.dtype), kind="ExternalInput").ap()

    w1 = np.asarray(inputs["W_top1"])
    emb_rows, pairs = F * D, F * (F - 1) // 2
    pair_row = np.full((F, F), -1)
    pair_row[np.triu_indices(F, k=1)] = np.arange(pairs)
    rest = np.full((NZ, P), -1)
    for r, (a, e) in enumerate(BLOCKS):
        rest[r, ROW0[r]:ROW0[r] + e * (e - a)] = pair_row[:e, a:e].reshape(-1)
    rest[NZ - 1, 1:AUX] = pairs + np.arange(NDENSE)
    rest[NZ - 1, 0] = pairs + NDENSE
    below = np.concatenate([w1[emb_rows:], np.asarray(inputs["b_top1"])[None, :], np.zeros((1, H1), w1.dtype)])
    args = [
        dram("ids_dram", np.asarray(inputs["ids"]).view(np.uint32)),
        [dram(f"tbl_{f}_dram", inputs[f"tbl_{f}"]) for f in range(F)],
        dram("w1_emb_dram", w1[:emb_rows]),
        dram("w1_rest_dram", below[rest.reshape(-1)]),
        dram("w2_dram", inputs["W_top2"]),
        dram("b2_dram", np.asarray(inputs["b_top2"])),
        dram("w3_dram", np.asarray(inputs["W_top3"]).reshape(H2)),
        dram("dense_t_dram", np.asarray(inputs["dense_ctx"]).T),
        [nc.dram_tensor(f"scratch{r}_dram", (P, (e - a) * QUAD), mybir.dt.float32, kind="Internal").ap()
         for r, (a, e) in enumerate(BLOCKS)],
    ]
    out = nc.dram_tensor("out_dram", (B, 1), mybir.dt.float32, kind="ExternalOutput").ap()
    build(nc, *args, out.rearrange("(t p) o -> p (t o)", p=P))
    r = run(nc, [arrays], core_ids=[0])
    return r.results[0]["out_dram"]
```
